# Optimizing a Trainium2 kernel written in Bass

```python
import numpy as np
import jax
import jax.numpy as jnp

def _softmax(x, axis=-1):
    return jax.nn.softmax(x, axis=axis)

def _gelu(x):
    return jax.nn.gelu(x, approximate=True)

def _silu(x):
    return jax.nn.silu(x)

def _sigmoid(x):
    return jax.nn.sigmoid(x)

def _layernorm(x, axis=-1, eps=1e-05):
    m = jnp.mean(x, axis=axis, keepdims=True)
    v = jnp.var(x, axis=axis, keepdims=True)
    return (x - m) / jnp.sqrt(v + eps)

def _scatter_add(tgt, idx, src, axis=0):
    return tgt.at[idx].add(src)

def _segment_sum(src, seg, n):
    return jax.ops.segment_sum(src, seg, n)
kernel_name = 'mk_adaln_ffn_d1_seqx_r4_b45fbd'

def setup_inputs(seed: int=0):
    np.random.seed(seed)
    _w = jnp.asarray

    def _rec_inputs():
        import jax
        import jax.numpy as jnp
        _rk = jax.random.key(seed)
        x = -0.000125 + 0.9999 * jax.random.normal(jax.random.fold_in(_rk, 1), (8, 256, 1024), jnp.float32)
        _lenS = 256 - jax.random.randint(jax.random.fold_in(_rk, 7), (8,), 0, max(1, 256 // 4) + 1, jnp.int32)
        _lenS2 = 256 - jax.random.randint(jax.random.fold_in(_rk, 8), (8,), 0, max(1, 256 // 4) + 1, jnp.int32)
        itok_B_0_23 = jax.random.randint(jax.random.fold_in(_rk, 11), (8,), 0, 24, jnp.int32)
        return (x, itok_B_0_23)
    x, itok_B_0_23 = _rec_inputs()

    def _L0_cond_setup():
        import jax, jax.numpy as jnp
        import numpy as np
        R = 16
        ALPHA = 32
        SCALING = ALPHA / R
        SLOTS = 32
        IN_F = 1024
        OUT_F = 1024
        B, T = (8, 256)
        key = jax.random.key(seed)
        k1, k2, k3, k4, k5, k6 = jax.random.split(key, 6)
        x = jax.random.normal(k1, (B, T, IN_F), dtype=jnp.float32)
        adapter_mapping = jax.random.randint(k2, (B,), 0, SLOTS, dtype=jnp.int32)
        W = jax.random.normal(k3, (OUT_F, IN_F), dtype=jnp.float32) * 0.02
        b = jax.random.normal(k4, (OUT_F,), dtype=jnp.float32) * 0.02
        lora_As = jax.random.normal(k5, (SLOTS, IN_F, R), dtype=jnp.float32) * 0.02
        lora_Bs = jax.random.normal(k6, (SLOTS, R, OUT_F), dtype=jnp.float32) * 0.02
        return {'x': x, 'adapter_mapping': adapter_mapping, 'W': W, 'b': b, 'lora_As': lora_As, 'lora_Bs': lora_Bs}
    _L0_cond_all = _L0_cond_setup()
    _L0_cond_in = {k: v for k, v in _L0_cond_all.items() if k in ('W', 'b', 'lora_As', 'lora_Bs')}
    del _L0_cond_all

    def _L0_ffn_setup():
        import jax, jax.numpy as jnp
        import numpy as np
        GROUP = 64

        def dequantize(W_q, scale, zero):
            out, half = W_q.shape
            hi = W_q >> 4 & 15
            lo = W_q & 15
            w = jnp.stack([hi, lo], axis=-1).reshape(out, half * 2).astype(scale.dtype)
            w = w.reshape(out, -1, GROUP)
            w = (w - zero[:, :, None]) * scale[:, :, None]
            return w.reshape(out, half * 2)
        key = jax.random.key(seed)
        ks = jax.random.split(key, 10)
        hidden, inter = (1024, 2752)
        B, S = (4, 256)
        x = jax.random.normal(ks[0], (B, S, hidden), dtype=jnp.float32)
        gate_Wq = jax.random.randint(ks[1], (inter, hidden // 2), 0, 64, dtype=jnp.int32)
        up_Wq = jax.random.randint(ks[2], (inter, hidden // 2), 0, 64, dtype=jnp.int32)
        down_Wq = jax.random.randint(ks[3], (hidden, inter // 2), 0, 64, dtype=jnp.int32)
        gate_scale = jax.random.uniform(ks[4], (inter, hidden // GROUP)) * 0.01 + 0.0001
        gate_zero = jax.random.uniform(ks[5], (inter, hidden // GROUP)) * 15.0
        up_scale = jax.random.uniform(ks[6], (inter, hidden // GROUP)) * 0.01 + 0.0001
        up_zero = jax.random.uniform(ks[7], (inter, hidden // GROUP)) * 15.0
        down_scale = jax.random.uniform(ks[8], (hidden, inter // GROUP)) * 0.01 + 0.0001
        down_zero = jax.random.uniform(ks[9], (hidden, inter // GROUP)) * 15.0
        return {'x': x, 'gate_Wq': gate_Wq, 'up_Wq': up_Wq, 'down_Wq': down_Wq, 'gate_scale': gate_scale, 'gate_zero': gate_zero, 'up_scale': up_scale, 'up_zero': up_zero, 'down_scale': down_scale, 'down_zero': down_zero}
    _L0_ffn_all = _L0_ffn_setup()
    _L0_ffn_in = {k: v for k, v in _L0_ffn_all.items() if k in ('gate_Wq', 'up_Wq', 'down_Wq', 'gate_scale', 'gate_zero', 'up_scale', 'up_zero', 'down_scale', 'down_zero')}
    del _L0_ffn_all
    return {'x': x, 'itok_B_0_23': itok_B_0_23, 'L0_cond_W': _L0_cond_in['W'], 'L0_cond_b': _L0_cond_in['b'], 'L0_cond_lora_As': _L0_cond_in['lora_As'], 'L0_cond_lora_Bs': _L0_cond_in['lora_Bs'], 'L0_ffn_gate_Wq': _L0_ffn_in['gate_Wq'], 'L0_ffn_up_Wq': _L0_ffn_in['up_Wq'], 'L0_ffn_down_Wq': _L0_ffn_in['down_Wq'], 'L0_ffn_gate_scale': _L0_ffn_in['gate_scale'], 'L0_ffn_gate_zero': _L0_ffn_in['gate_zero'], 'L0_ffn_up_scale': _L0_ffn_in['up_scale'], 'L0_ffn_up_zero': _L0_ffn_in['up_zero'], 'L0_ffn_down_scale': _L0_ffn_in['down_scale'], 'L0_ffn_down_zero': _L0_ffn_in['down_zero']}

def reference(x, itok_B_0_23, L0_cond_W, L0_cond_b, L0_cond_lora_As, L0_cond_lora_Bs, L0_ffn_gate_Wq, L0_ffn_up_Wq, L0_ffn_down_Wq, L0_ffn_gate_scale, L0_ffn_gate_zero, L0_ffn_up_scale, L0_ffn_up_zero, L0_ffn_down_scale, L0_ffn_down_zero):
    import jax
    import jax.numpy as jnp

    def _L0_cond_ref(x, adapter_mapping, W, b, lora_As, lora_Bs):
        import jax, jax.numpy as jnp
        import numpy as np
        R = 16
        ALPHA = 32
        SCALING = ALPHA / R
        SLOTS = 32
        IN_F = 1024
        OUT_F = 1024
        B, T = (8, 256)
        base_out = jnp.einsum('bti,oi->bto', x, W) + b
        A = lora_As[adapter_mapping]
        Bm = lora_Bs[adapter_mapping]
        lora_h = jnp.einsum('bti,bir->btr', x, A)
        lora_out = jnp.einsum('btr,bro->bto', lora_h, Bm)
        return base_out + lora_out * SCALING

    def _L0_ffn_ref(x, gate_Wq, up_Wq, down_Wq, gate_scale, gate_zero, up_scale, up_zero, down_scale, down_zero):
        import jax, jax.numpy as jnp
        import numpy as np
        GROUP = 64

        def dequantize(W_q, scale, zero):
            out, half = W_q.shape
            hi = W_q >> 4 & 15
            lo = W_q & 15
            w = jnp.stack([hi, lo], axis=-1).reshape(out, half * 2).astype(scale.dtype)
            w = w.reshape(out, -1, GROUP)
            w = (w - zero[:, :, None]) * scale[:, :, None]
            return w.reshape(out, half * 2)
        Wg = dequantize(gate_Wq, gate_scale, gate_zero)
        Wu = dequantize(up_Wq, up_scale, up_zero)
        Wd = dequantize(down_Wq, down_scale, down_zero)
        g = jnp.einsum('bsh,ih->bsi', x, Wg)
        u = jnp.einsum('bsh,ih->bsi', x, Wu)
        h = jax.nn.silu(g) * u
        return jnp.einsum('bsi,hi->bsh', h, Wd)
    x = x + _L0_ffn_ref(_L0_cond_ref(x, itok_B_0_23, L0_cond_W, L0_cond_b, L0_cond_lora_As, L0_cond_lora_Bs), L0_ffn_gate_Wq, L0_ffn_up_Wq, L0_ffn_down_Wq, L0_ffn_gate_scale, L0_ffn_gate_zero, L0_ffn_up_scale, L0_ffn_up_zero, L0_ffn_down_scale, L0_ffn_down_zero)
    return x

_drawn_inputs = setup_inputs


def setup_inputs(seed=0):
    import zlib

    import numpy as np

    out = dict(_drawn_inputs(seed))
    spreads = {}
    factors = {'L0_cond_b': 8.0}
    for name, (base, spread) in spreads.items():
        noise = np.random.default_rng([zlib.crc32(name.encode()), seed]).standard_normal(out[name].shape)
        drawn = base * np.exp(spread * noise) if base else spread * noise
        out[name] = jnp.asarray(drawn.astype(out[name].dtype))
    for name, factor in factors.items():
        out[name] = (out[name] * factor).astype(out[name].dtype)
    return out
```

```python
from contextlib import ExitStack

import concourse.bass as bass
from concourse import mybir

F32 = mybir.dt.float32
F32R = mybir.dt.float32r
I32 = mybir.dt.int32
ALU = mybir.AluOpType
ACT = mybir.ActivationFunctionType
ds = bass.ds

P = 128
D = 1024
KT = D // P
MB = KT // 2
NT = 512
BT = 256
R = 16
HALVES = 2
TN = 2
HT = TN * NT
INTER = 2752
PAIRS = INTER // (2 * P)
NPAIR = PAIRS + 1
TAIL = INTER - PAIRS * 2 * P
LASTM = TAIL - P
TAILJ = TAIL // 2
GROUPS = 16
LORA_SCALE = 2.0
SLOTS = 32

X_CHUNKS = 4
UNITS = TN * KT
GU = NPAIR * 4
UP = GU - TN
DN = TN * KT
DH = NPAIR * DN
SP_PAIR = 6
STEPS = 4 + PAIRS * SP_PAIR + 2
CR = 4


def build(nc, xT, idx, wT, bias, loraA, loraB, guq, gusz, dq, dsz, out):
    ctx = ExitStack()
    with ctx:
        def sb(name, shape, dt):
            return ctx.enter_context(nc.sbuf_tensor(name, shape, dt))

        def pb(name, shape):
            return ctx.enter_context(nc.psum_tensor(name, shape, F32))

        def sem(name):
            return ctx.enter_context(nc.semaphore(name))

        Ch = sb("Ch", [P, KT, HT], F32R)
        Cl = sb("Cl", [P, KT, HT], F32R)
        acc = sb("acc", [P, KT, HT], F32)
        Wh = sb("Wh", [P, 2, 2 * D], F32R)
        Wl = sb("Wl", [P, 2, 2 * D], F32R)
        Hh = sb("Hh", [P, 2 * TN * HT], F32R)
        Hl = sb("Hl", [P, 2 * TN * HT], F32R)
        raw = sb("raw", [P, 2, D], I32)
        sz = sb("sz", [P, 2, 2, 2, P], F32)
        rawd = sb("rawd", [P, D], I32)
        szd = sb("szd", [P, 2, D], F32)
        tmp = sb("tmp", [P, 2, D], F32)
        sg = sb("sg", [P, 2, NT], F32)
        hf = sb("hf", [P, 2, NT], F32)
        lh = sb("lh", [P, NT], F32R)
        araw = sb("araw", [P, 2, KT * R], F32)
        Ah = sb("Ah", [P, 2, KT * R], F32R)
        Al = sb("Al", [P, 2, KT * R], F32R)
        bcol = sb("bcol", [P, KT], F32)

        pg = pb("pg", [P, 2, 2, NT])
        pd = pb("pd", [P, 4, NT])

        x_in = [sem(f"x_in{q}") for q in range(2)]
        w_in = [sem(f"w_in{q}") for q in range(2)]
        gu_in = [sem(f"gu_in{q}") for q in range(2)]
        d_in = sem("d_in")
        lora_in = sem("lora_in")
        acc_in = [sem(f"acc_in{n}") for n in range(TN)]
        bias_in = sem("bias_in")
        stored = sem("stored")
        szd_zero = sem("szd_zero")
        lh_zero = sem("lh_zero")
        x_high = sem("x_high")
        a_high = sem("a_high")
        b_high = sem("b_high")
        w_high = sem("w_high")
        lh_high = sem("lh_high")
        c_high = sem("c_high")
        q_high = sem("q_high")
        h_high = sem("h_high")
        sig_done = sem("sig_done")
        u_copied = sem("u_copied")
        x_split = sem("x_split")
        a_split = sem("a_split")
        b_split = sem("b_split")
        w_split = sem("w_split")
        lh_split = sem("lh_split")
        c_split = sem("c_split")
        gu_split = sem("gu_split")
        wd_split = sem("wd_split")
        h_split = sem("h_split")
        unpacked = sem("unpacked")
        centered = sem("centered")
        scaled = sem("scaled")
        silu_done = sem("silu_done")
        hf_done = sem("hf_done")
        added = sem("added")
        lora_mm = sem("lora_mm")
        c_mm = sem("c_mm")
        g_mm = sem("g_mm")
        u_mm = sem("u_mm")
        d_mm = sem("d_mm")

        block = ctx.enter_context(nc.Block())

        def f(ap):
            return ap.bitcast(F32)

        def x_part(t, c):
            return t[:, c * 2 * NT:(c + 1) * 2 * NT]

        def gu_part(t, slot, v):
            return t[:, slot, :].rearrange("p (g v n) -> p g v n", g=2, v=2)[:, :, v, :]

        def wd_part(t, tile):
            return t[:, TN * HT + tile * D:TN * HT + (tile + 1) * D]

        def h_part(t, tile, n, p0=0, p1=P):
            return t[p0:p1, tile * HT + n * NT:tile * HT + (n + 1) * NT]

        def step(j, i):
            return 4 + j * SP_PAIR + i

        @block.sync
        def _(sp):
            sp.dma_start(bcol[:, :], bias).then_inc(bias_in, 16)

            def load_gate_up(half, T, slot):
                sp.dma_start(raw[:, slot, :], guq[ds(T, 1), :, :].rearrange("t p n -> (t p) n"))\
                    .then_inc(gu_in[slot], 16)
                sp.dma_start(sz[:, slot, :, :, :].rearrange("p z g n -> p (z g n)"),
                             gusz[ds(T, 1), :, :].rearrange("t g n -> (t g) n").unsqueeze(1)
                             .broadcast_to([GROUPS, P // GROUPS, 4 * P])).then_inc(gu_in[slot], 16)

            def load_down(T):
                sp.dma_start(rawd[:, :], dq[ds(T, 1), :, :].rearrange("t p n -> (t p) n")).then_inc(d_in, 16)
                sp.dma_start(szd[:, :, :].rearrange("p z n -> p (z n)"),
                             dsz[ds(T, 1), :, :].rearrange("t g n -> (t g) n").unsqueeze(1)
                             .broadcast_to([4, P // 4, 2 * D])).then_inc(d_in, 16)

            with sp.Fori(0, HALVES) as half:
                for n in range(TN):
                    nt = half * TN + n
                    adapters = [sp.value_load(idx[0:1, ds(nt * 2 + b, 1)], min_val=0, max_val=SLOTS - 1)
                                for b in range(2)]

                    def load_x(c):
                        if c >= 2 or n > 0:
                            sp.wait_ge(x_split, half * 2 * X_CHUNKS + n * X_CHUNKS + c - 1)
                        else:
                            sp.wait_ge(wd_split, half * 2 * NPAIR + CR)
                        sp.dma_start(tmp[:, c % 2, :],
                                     xT[ds(nt, 1), :, c * 2 * NT:(c + 1) * 2 * NT].rearrange("t p n -> (t p) n"))\
                            .then_inc(x_in[c % 2], 16)

                    def load_w(o):
                        i = n * KT + o
                        if i >= 2:
                            sp.wait_ge(w_split, half * UNITS + i - 1)
                        else:
                            sp.wait_ge(scaled, half * STEPS + CR)
                        sp.dma_start(f(raw[:, o % 2, :]), wT[o, :, :]).then_inc(w_in[o % 2], 16)

                    load_x(0)
                    load_x(1)
                    if n > 0:
                        sp.wait_ge(a_split, half * TN + n)
                        sp.wait_ge(b_split, half * TN + n)
                    else:
                        sp.wait_ge(szd_zero, half + 1)
                    for b in range(2):
                        slot = adapters[b]
                        sp.dma_start(araw[:, b, :], loraA[ds(slot, 1), :, :].rearrange("s p n -> (s p) n"))\
                            .then_inc(lora_in, 16)
                        for r in (0, 32, 64):
                            sp.dma_start(szd[r:r + R, b, :], loraB[ds(slot, 1), :, :].rearrange("s p n -> (s p) n"))\
                                .then_inc(lora_in, 16)
                    load_w(0)
                    load_w(1)
                    load_x(2)
                    load_x(3)
                    for o in range(2, KT):
                        load_w(o)
                for t in range(2):
                    sp.wait_ge(w_split, half * UNITS + UNITS - 1 + t)
                    load_gate_up(half, t, t)
                sp.wait_ge(b_split, half * TN + TN)
                load_down(0)
                sp.wait_ge(stored, half * 64 + 16)
                for n in range(TN):
                    sp.dma_start(acc[:, :, n * NT:(n + 1) * NT],
                                 xT[ds(half * TN + n, 1), :, :].rearrange("t p (k c) -> (t p) k c", k=KT))\
                        .then_inc(acc_in[n], 16)
                with sp.Fori(0, PAIRS) as j:
                    for t in range(2):
                        sp.wait_ge(scaled, half * STEPS + j * SP_PAIR + 2 * t + 2 + CR)
                        load_gate_up(half, j * 2 + 2 + t, t)
                    sp.wait_ge(scaled, half * STEPS + step(j, 2) + CR)
                    load_down(j + 1)
                sp.wait_ge(scaled, half * STEPS + step(PAIRS, 1) + CR)
                load_down(NPAIR)

        @block.gpsimd
        def _(pool):
            pool.memset(f(lh[:, :]), 0.0).then_inc(lh_zero, 1)

        @block.scalar
        def _(act):
            act.sem_inc(stored, 16)
            act.wait_ge(bias_in, 16)
            act.wait_ge(lh_zero, 1)

            def round_to(dst, src, done):
                act.activation(dst, src, ACT.Copy).then_inc(done, 1)

            with act.Fori(0, HALVES) as half:
                for n in range(TN):
                    def round_x(c):
                        if c == 0 and n == 0:
                            act.wait_ge(d_mm, half * DH + CR)
                        elif c == 0:
                            act.wait_ge(c_mm, half * UNITS + n * KT)
                        act.wait_ge(x_in[c % 2], (half * 2 * TN + n * 2 + c // 2 + 1) * 16)
                        round_to(x_part(Hh, c), tmp[:, c % 2, :], x_high)

                    def round_w(o):
                        i = n * KT + o
                        if i >= 2:
                            act.wait_ge(c_mm, half * UNITS + i - 1)
                        act.wait_ge(w_in[o % 2], (half * KT + i // 2 + 1) * 16)
                        round_to(Wh[:, o % 2, 0:D], f(raw[:, o % 2, :]), w_high)

                    def evac(o, m):
                        act.wait_ge(c_mm, half * UNITS + m * KT + o + 1)
                        act.activation(Ch[:, o, m * NT:(m + 1) * NT], pd[:, o % 4, :], ACT.Identity,
                                       bias=bcol[:, o:o + 1]).then_inc(c_high, 1)

                    round_x(0)
                    if n > 0:
                        evac(KT - 1, n - 1)
                    round_x(1)
                    act.wait_ge(lora_in, (half * TN + n + 1) * 128)
                    round_to(Ah[:, :, :], araw[:, :, :], a_high)
                    round_x(2)
                    round_x(3)
                    round_w(0)
                    round_w(1)
                    for b in range(2):
                        round_to(Wh[0:96, b, D:2 * D], szd[0:96, b, :], b_high)
                    act.wait_ge(lora_mm, half * TN + n + 1)
                    for r in (0, 64):
                        act.activation(lh[r:r + R, :].rearrange("p (b n) -> p b n", b=2), pg[0:R, 0, :, 0:BT],
                                       ACT.Copy, scale=LORA_SCALE).then_inc(lh_high, 1)
                    for o in range(KT - 1):
                        evac(o, n)
                        if o + 2 < KT:
                            round_w(o + 2)

                def round_q(v, dst, src):
                    act.wait_ge(scaled, half * STEPS + v + 1 + CR)
                    round_to(dst, src, q_high)

                def round_gate_up(v0, t):
                    for v in range(2):
                        round_q(v0 + v, gu_part(Wh, t, v), tmp[:, v, :].rearrange("p (g n) -> p g n", g=2))

                def sigmoid(j, u):
                    act.wait_ge(g_mm, half * GU + j * 4 + u + 1)
                    act.activation(sg[:, u % 2, :], pg[:, u % 2, 0, :], ACT.Sigmoid).then_inc(sig_done, 1)

                def round_h(j, u):
                    act.wait_ge(hf_done, half * GU + j * 4 + u + 1)
                    round_to(h_part(Hh, u // 2, u % 2), hf[:, u % 2, :], h_high)

                act.wait_ge(c_mm, half * UNITS + UNITS)
                round_gate_up(0, 0)
                evac(KT - 1, TN - 1)
                round_gate_up(2, 1)

                with act.Fori(0, PAIRS) as j:
                    act.wait_ge(d_mm, half * DH + j * DN + CR)
                    round_q(step(j, 0), wd_part(Hh, 0), tmp[:, 0, :])
                    sigmoid(j, 0)
                    round_q(step(j, 1), wd_part(Hh, 1), tmp[:, 1, :])
                    round_h(j, 0)
                    sigmoid(j, 1)
                    round_h(j, 1)
                    act.wait_ge(u_mm, half * UP + j * 4 + 2)
                    round_gate_up(step(j, 2), 0)
                    sigmoid(j, 2)
                    round_h(j, 2)
                    sigmoid(j, 3)
                    round_h(j, 3)
                    act.wait_ge(u_mm, half * UP + j * 4 + 4)
                    round_gate_up(step(j, 4), 1)

                j = PAIRS
                act.wait_ge(d_mm, half * DH + j * DN + CR)
                round_q(step(j, 0), wd_part(Hh, 0), tmp[:, 0, :])
                sigmoid(j, 0)
                round_h(j, 0)
                round_q(step(j, 1), wd_part(Hh, 1), tmp[:, 1, :])
                sigmoid(j, 1)
                round_h(j, 1)
                for n in range(TN):
                    act.wait_ge(g_mm, half * GU + j * 4 + 2 + n + 1)
                    act.activation(sg[0:LASTM, n, :], pg[0:LASTM, n, 0, :], ACT.Sigmoid).then_inc(sig_done, 1)
                    act.activation(hf[0:LASTM, n, :], pg[LASTM:P, n, 0, :], ACT.Copy).then_inc(u_copied, 1)
                    act.wait_ge(hf_done, half * GU + j * 4 + 2 + n + 1)
                    round_to(h_part(Hh, 1, n, 0, LASTM), hf[0:LASTM, n, :], h_high)
                for n in range(TN):
                    for q in range(2):
                        act.wait_ge(added, half * DH + PAIRS * DN + n * KT + (q + 1) * 4 + CR)
                        act.dma_start(out[ds(half * TN + n, 1), :, q * 4 * NT:(q + 1) * 4 * NT]
                                      .rearrange("t p (k c) -> (t p) k c", k=4),
                                      acc[:, q * 4:(q + 1) * 4, n * NT:(n + 1) * NT]).then_inc(stored, 16)
            act.wait_ge(stored, HALVES * 64 + 16)

        @block.vector
        def _(dve):
            dve.sem_inc(scaled, CR)
            dve.sem_inc(wd_split, CR)
            dve.sem_inc(added, CR)
            dve.sem_inc(h_split, CR)

            dve.memset(szd[:, :, :], 0.0).then_inc(szd_zero, 1)

            def low(dst, src, high, done):
                dve.tensor_tensor(dst, src, high, ALU.subtract).then_inc(done, 1)

            with dve.Fori(0, HALVES) as half:
                def dequantise(v, parts, zeros, scales, shape, q, tmp_read):
                    dve.wait_ge(*tmp_read)
                    for i, (p0, p1, packed, high) in enumerate(parts):
                        dst = tmp[p0:p1, q, :].bitcast(I32)
                        if high:
                            ins = dve.tensor_scalar(dst, packed, 4, 15, ALU.arith_shift_right, ALU.bitwise_and)
                        else:
                            ins = dve.tensor_scalar(dst, packed, 15, None, ALU.bitwise_and)
                        if i == len(parts) - 1:
                            ins.then_inc(unpacked, 1)
                    dve.wait_ge(unpacked, half * STEPS + v + 1)
                    dve.tensor_tensor(shape(tmp[:, q, :]), shape(tmp[:, q, :].bitcast(I32)), zeros, ALU.subtract)\
                       .then_inc(centered, 1)
                    dve.wait_ge(centered, half * STEPS + v + 1)
                    dve.tensor_tensor(shape(tmp[:, q, :]), shape(tmp[:, q, :]), scales, ALU.mult).then_inc(scaled, 1)

                def dequantise_gate_up(v, slot, nib, landed, tmp_read):
                    if nib == 0:
                        dve.wait_ge(gu_in[slot], landed)
                    zs = [sz[:, slot, i, :, :].unsqueeze(2).broadcast_to([P, 2, MB, P]) for i in range(2)]
                    dequantise(v, [(0, P, raw[:, slot, :], nib == 0)], zs[0], zs[1],
                               lambda a: a.rearrange("p (g m c) -> p g m c", g=2, m=MB), nib, tmp_read)

                def low_gate_up(v, t, nib):
                    dve.wait_ge(q_high, half * STEPS + v + 1)
                    low(gu_part(Wl, t, nib), tmp[:, nib, :].rearrange("p (g n) -> p g n", g=2),
                        f(gu_part(Wh, t, nib)), gu_split)

                def low_wd(v, tile):
                    dve.wait_ge(q_high, half * STEPS + v + 1)
                    low(wd_part(Hl, tile), tmp[:, tile, :], f(wd_part(Hh, tile)), wd_split)

                def flat(a):
                    return a

                for n in range(TN):
                    def low_x(c):
                        dve.wait_ge(x_high, half * 2 * X_CHUNKS + n * X_CHUNKS + c + 1)
                        low(x_part(Hl, c), tmp[:, c % 2, :], f(x_part(Hh, c)), x_split)

                    def low_w(o):
                        dve.wait_ge(w_high, half * UNITS + n * KT + o + 1)
                        low(Wl[:, o % 2, 0:D], f(raw[:, o % 2, :]), f(Wh[:, o % 2, 0:D]), w_split)

                    def low_c(o, m):
                        dve.wait_ge(c_high, half * UNITS + m * KT + o + 1)
                        dve.scalar_tensor_tensor(Cl[:, o, m * NT:(m + 1) * NT], pd[:, o % 4, :],
                                                 bcol[:, o:o + 1], f(Ch[:, o, m * NT:(m + 1) * NT]),
                                                 op0=ALU.add, op1=ALU.subtract).then_inc(c_split, 1)

                    low_x(0)
                    if n > 0:
                        low_c(KT - 1, n - 1)
                    low_x(1)
                    dve.wait_ge(a_high, half * TN + n + 1)
                    low(Al[:, :, :], araw[:, :, :], f(Ah[:, :, :]), a_split)
                    low_x(2)
                    low_x(3)
                    low_w(0)
                    low_w(1)
                    dve.wait_ge(b_high, (half * TN + n + 1) * 2)
                    low(Wh[64:64 + R, :, D:2 * D], szd[64:64 + R, :, :], f(Wh[64:64 + R, :, D:2 * D]), b_split)
                    dve.wait_ge(lh_high, (half * TN + n + 1) * 2)
                    dve.scalar_tensor_tensor(lh[32:32 + R, :].rearrange("p (b n) -> p b n", b=2),
                                             pg[0:R, 0, :, 0:BT], LORA_SCALE,
                                             f(lh[0:R, :]).rearrange("p (b n) -> p b n", b=2),
                                             op0=ALU.mult, op1=ALU.subtract).then_inc(lh_split, 1)
                    for o in range(KT - 1):
                        low_c(o, n)
                        if o + 2 < KT:
                            low_w(o + 2)

                first = (half * NPAIR + 1) * 32
                dequantise_gate_up(0, 0, 0, first, (x_split, (half + 1) * 2 * X_CHUNKS - 1))
                dequantise_gate_up(1, 0, 1, first, (x_split, (half + 1) * 2 * X_CHUNKS))
                low_gate_up(0, 0, 0)
                low_gate_up(1, 0, 1)
                low_c(KT - 1, TN - 1)
                dequantise_gate_up(2, 1, 0, first, (gu_split, half * GU + 1))
                dequantise_gate_up(3, 1, 1, first, (gu_split, half * GU + 2))
                low_gate_up(2, 1, 0)
                low_gate_up(3, 1, 1)

                def make_h(j, u):
                    s = u % 2
                    dve.wait_ge(sig_done, half * GU + j * 4 + u + 1)
                    dve.tensor_tensor(sg[:, s, :], pg[:, s, 0, :], sg[:, s, :], ALU.mult).then_inc(silu_done, 1)
                    dve.wait_ge(u_mm, half * UP + j * 4 + u + 1)
                    dve.wait_ge(silu_done, half * GU + j * 4 + u + 1)
                    dve.tensor_tensor(hf[:, s, :], pg[:, s, 1, :], sg[:, s, :], ALU.mult).then_inc(hf_done, 1)

                def low_h(j, u):
                    dve.wait_ge(h_high, half * GU + j * 4 + u + 1)
                    low(h_part(Hl, u // 2, u % 2), hf[:, u % 2, :], f(h_part(Hh, u // 2, u % 2)), h_split)

                def add(j, n, m):
                    i = n * KT + m
                    if m == 0:
                        dve.wait_ge(acc_in[n], (half + 1) * 16)
                    dve.wait_ge(d_mm, half * DH + j * DN + i + 1 + CR)
                    a = acc[:, m, n * NT:(n + 1) * NT]
                    dve.tensor_tensor(a, a, pd[:, i % 4, :], ALU.add).then_inc(added, 1)

                with dve.Fori(0, PAIRS) as j:
                    dve.wait_ge(d_in, (half * (NPAIR + 1) + j + 1) * 32)
                    dequantise(step(j, 0), [(0, P, rawd[:, :], True)], szd[:, 0, :], szd[:, 1, :], flat, 0,
                               (gu_split, half * GU + j * 4 + 3))
                    dequantise(step(j, 1), [(0, P, rawd[:, :], False)], szd[:, 0, :], szd[:, 1, :], flat, 1,
                               (gu_split, half * GU + j * 4 + 4))
                    low_wd(step(j, 0), 0)
                    low_wd(step(j, 1), 1)
                    make_h(j, 0)
                    low_h(j, 0)
                    landed = (half * NPAIR + j + 2) * 32
                    dequantise_gate_up(step(j, 2), 0, 0, landed, (wd_split, half * 2 * NPAIR + 2 * j + 1 + CR))
                    dequantise_gate_up(step(j, 3), 0, 1, landed, (wd_split, half * 2 * NPAIR + 2 * j + 2 + CR))
                    make_h(j, 1)
                    low_h(j, 1)
                    low_gate_up(step(j, 2), 0, 0)
                    low_gate_up(step(j, 3), 0, 1)
                    dequantise_gate_up(step(j, 4), 1, 0, landed, (gu_split, half * GU + j * 4 + 5))
                    dequantise_gate_up(step(j, 5), 1, 1, landed, (gu_split, half * GU + j * 4 + 6))
                    make_h(j, 2)
                    low_h(j, 2)
                    make_h(j, 3)
                    low_h(j, 3)
                    for n in range(TN):
                        for m in range(KT):
                            add(j, n, m)
                            if n == 0 and m < 2:
                                low_gate_up(step(j, 4 + m), 1, m)

                j = PAIRS
                dve.wait_ge(d_in, (half * (NPAIR + 1) + j + 1) * 32)
                dequantise(step(j, 0), [(0, TAILJ, rawd[0:TAILJ, :], True), (TAILJ, P, rawd[TAILJ:P, :], False)],
                           szd[:, 0, :], szd[:, 1, :], flat, 0, (gu_split, half * GU + GU - 1))
                low_wd(step(j, 0), 0)
                make_h(j, 0)
                low_h(j, 0)
                dve.wait_ge(d_in, (half * (NPAIR + 1) + j + 2) * 32)
                dequantise(step(j, 1), [(0, P, rawd[:, :], False)], szd[:, 0, :], szd[:, 1, :], flat, 1,
                           (gu_split, half * GU + GU))
                low_wd(step(j, 1), 1)
                make_h(j, 1)
                low_h(j, 1)
                dve.wait_ge(scaled, half * STEPS + STEPS + CR)
                dve.memset(szd[:, :, :], 0.0).then_inc(szd_zero, 1)
                for n in range(TN):
                    i = half * GU + j * 4 + 2 + n + 1
                    dve.wait_ge(sig_done, i)
                    dve.tensor_tensor(sg[0:LASTM, n, :], pg[0:LASTM, n, 0, :], sg[0:LASTM, n, :], ALU.mult)\
                       .then_inc(silu_done, 1)
                    dve.wait_ge(silu_done, i)
                    dve.wait_ge(u_copied, half * TN + n + 1)
                    dve.tensor_tensor(hf[0:LASTM, n, :], hf[0:LASTM, n, :], sg[0:LASTM, n, :], ALU.mult)\
                       .then_inc(hf_done, 1)
                    dve.wait_ge(h_high, i)
                    low(h_part(Hh, 1, n, LASTM, P), hf[0:LASTM, n, :], f(h_part(Hh, 1, n, 0, LASTM)), h_split)
                for n in range(TN):
                    for m in range(KT):
                        add(j, n, m)

        @block.tensor
        def _(pe):
            pe.sem_inc(d_mm, CR)

            with pe.Fori(0, HALVES) as half:
                for n in range(TN):
                    pe.wait_ge(h_split, half * GU + CR)
                    for k in range(KT):
                        if k % 2 == 0:
                            pe.wait_ge(x_split, half * 2 * X_CHUNKS + n * X_CHUNKS + k // 2 + 1)
                        if k == 0:
                            pe.wait_ge(a_split, half * TN + n + 1)
                        for b in range(2):
                            o = pg[0:R, 0, b, 0:BT]
                            cols = slice(k * NT + b * BT, k * NT + (b + 1) * BT)
                            ah, al = (t[:, b, k * R:(k + 1) * R] for t in (Ah, Al))
                            pe.matmul(o, ah, Hh[:, cols], start=(k == 0), stop=False)
                            pe.matmul(o, ah, Hl[:, cols], start=False, stop=False)
                            last = pe.matmul(o, al, Hh[:, cols], start=False, stop=(k == KT - 1))
                    last.then_inc(lora_mm, 1)
                    for m in range(KT):
                        i = n * KT + m
                        if i < 4:
                            pe.wait_ge(added, half * DH + CR)
                        else:
                            pe.wait_ge(c_split, half * UNITS + i - 3)
                        pe.wait_ge(w_split, half * UNITS + i + 1)
                        o = pd[:, m % 4, :]
                        for k in range(KT):
                            wh, wl = (t[:, m % 2, k * P:(k + 1) * P] for t in (Wh, Wl))
                            xs = slice(k * NT, (k + 1) * NT)
                            if k == KT - 1:
                                if m == 0:
                                    pe.wait_ge(b_split, half * TN + n + 1)
                                    pe.wait_ge(lh_split, half * TN + n + 1)
                                for b in range(2):
                                    pe.matmul(pd[:, m % 4, b * BT:(b + 1) * BT], Wh[0:96, b, D + m * P:D + (m + 1) * P],
                                              lh[0:96, b * BT:(b + 1) * BT], start=False, stop=False)
                            pe.matmul(o, wh, Hh[:, xs], start=(k == 0), stop=False)
                            pe.matmul(o, wh, Hl[:, xs], start=False, stop=False)
                            last = pe.matmul(o, wl, Hh[:, xs], start=False, stop=(k == KT - 1))
                        last.then_inc(c_mm, 1)

                def project(j, t, n, g):
                    o = pg[:, n, g, :]
                    for k in range(KT):
                        if g == 0 and n == 0 and k % MB == 0:
                            pe.wait_ge(gu_split, half * GU + j * 4 + t * 2 + k // MB + 1)
                        wh, wl = (w[:, t, g * D + k * P:g * D + (k + 1) * P] for w in (Wh, Wl))
                        cs = slice(n * NT, (n + 1) * NT)
                        pe.matmul(o, wh, Ch[:, k, cs], start=(k == 0), stop=False)
                        pe.matmul(o, wh, Cl[:, k, cs], start=False, stop=False)
                        last = pe.matmul(o, wl, Ch[:, k, cs], start=False, stop=(k == KT - 1))
                    return last

                def gate_up_unit(j, t, n):
                    u = t * TN + n
                    pe.wait_ge(h_split, half * GU + j * 4 + u - 1 + CR)
                    if t == 0:
                        pe.wait_ge(c_split, half * UNITS + (n + 1) * KT)
                    project(j, t, n, 0).then_inc(g_mm, 1)
                    project(j, t, n, 1).then_inc(u_mm, 1)

                def down(j, terms):
                    for n in range(TN):
                        pe.wait_ge(h_split, half * GU + j * 4 + 3 + n + CR)
                        if n == 0:
                            pe.wait_ge(wd_split, half * 2 * NPAIR + j * 2 + 2 + CR)
                        for m in range(KT):
                            i = n * KT + m
                            pe.wait_ge(added, half * DH + j * DN + i - 3 + CR)
                            for a, (w, h, tile) in enumerate(terms):
                                lo = TN * HT + tile * D + m * P
                                last = pe.matmul(pd[:, i % 4, :], w[:, lo:lo + P], h_part(h, tile, n),
                                                 start=(a == 0), stop=(a == len(terms) - 1))
                            last.then_inc(d_mm, 1)

                with pe.Fori(0, PAIRS) as j:
                    for t in range(2):
                        for n in range(TN):
                            gate_up_unit(j, t, n)
                    down(j, [(w, h, t) for t in range(2) for w, h in ((Hh, Hh), (Hh, Hl), (Hl, Hh))])

                j = PAIRS
                for n in range(TN):
                    gate_up_unit(j, 0, n)
                for n in range(TN):
                    pe.wait_ge(h_split, half * GU + j * 4 + 2 + n - 1 + CR)
                    project(j, 1, n, 0).then_inc(g_mm, 1)
                down(j, [(Hh, Hh, 0), (Hh, Hl, 0), (Hl, Hh, 0), (Hh, Hh, 1), (Hl, Hh, 1)])


def kernel(x, itok_B_0_23, L0_cond_W, L0_cond_b, L0_cond_lora_As, L0_cond_lora_Bs,
           L0_ffn_gate_Wq, L0_ffn_up_Wq, L0_ffn_down_Wq, L0_ffn_gate_scale, L0_ffn_gate_zero,
           L0_ffn_up_scale, L0_ffn_up_zero, L0_ffn_down_scale, L0_ffn_down_zero):
    import numpy as np
    import concourse.bacc as bacc
    from concourse.bass_utils import run_bass_kernel_spmd

    def c_rows(a):
        a = a.reshape(*a.shape[:-1], GROUPS, MB, 8, 2)
        lead = tuple(range(a.ndim - 4))
        return a.transpose(*lead, *(len(lead) + i for i in (3, 1, 0, 2)))

    def inter_tiles(a):
        main = a[:PAIRS * 2 * P].reshape(PAIRS, P, 2, -1).transpose(0, 2, 1, 3).reshape(2 * PAIRS, P, -1)
        tail = a[PAIRS * 2 * P:].reshape(TAILJ, 2, -1)
        return [*main, np.concatenate([tail[:, 0], tail[:P - TAILJ, 1]]), tail[P - TAILJ:, 1]]

    def gate_up(g, u):
        g, u = inter_tiles(g), inter_tiles(u)
        last = np.concatenate([g[-1], u[-1]])
        return np.stack([np.stack([a, b]) for a, b in zip(g[:-1], u[:-1])] + [np.stack([last, last])])

    x = np.asarray(x)
    xT = x.reshape(HALVES * TN, NT, KT, P).transpose(0, 3, 2, 1).reshape(HALVES * TN, P, KT * NT)
    W = np.asarray(L0_cond_W)
    wT = c_rows(W.T).reshape(KT, P, 2 * MB, P).transpose(2, 1, 0, 3).reshape(KT, P, D)
    bias = c_rows(np.asarray(L0_cond_b)).reshape(KT, P).T
    loraA = np.asarray(L0_cond_lora_As).reshape(SLOTS, KT, P, R).transpose(0, 2, 1, 3).reshape(SLOTS, P, KT * R)
    loraB = c_rows(np.asarray(L0_cond_lora_Bs)).reshape(SLOTS, R, D)
    guq = gate_up(np.asarray(L0_ffn_gate_Wq), np.asarray(L0_ffn_up_Wq))
    guq = guq.reshape(-1, 2, P, GROUPS, MB, 8).transpose(0, 3, 5, 1, 4, 2).reshape(-1, P, D)
    gz = gate_up(np.asarray(L0_ffn_gate_zero), np.asarray(L0_ffn_up_zero))
    gs = gate_up(np.asarray(L0_ffn_gate_scale), np.asarray(L0_ffn_up_scale))
    gusz = np.stack([gz, gs], axis=1).transpose(0, 4, 1, 2, 3).reshape(-1, GROUPS, 4 * P)
    dqT = np.asarray(L0_ffn_down_Wq).T
    tail = dqT[PAIRS * P:]
    dq = np.concatenate([dqT[:PAIRS * P].reshape(PAIRS, P, D),
                         np.concatenate([tail, tail[:P - TAILJ]])[None],
                         np.concatenate([tail[P - TAILJ:], tail[P - TAILJ:]])[None]])
    z, s = np.asarray(L0_ffn_down_zero).T, np.asarray(L0_ffn_down_scale).T
    zs = np.stack([z, s], axis=1).reshape(-1, 2 * D)
    t = 4 * PAIRS
    dsz = np.concatenate([zs[:t].reshape(PAIRS, 4, 2 * D), np.stack([zs[t], zs[t + 1], zs[t + 2], zs[t]])[None],
                          np.stack([zs[t + 1], zs[t + 2], zs[t + 1], zs[t + 2]])[None]])

    nc = bacc.Bacc("TRN2", target_bir_lowering=False, num_devices=1)
    arrays = {"xT": xT, "idx": np.asarray(itok_B_0_23).reshape(1, -1), "wT": wT, "bias": bias, "loraA": loraA,
              "loraB": loraB, "guq": guq, "gusz": gusz, "dq": dq, "dsz": dsz}
    arrays = {n: np.ascontiguousarray(a) for n, a in arrays.items()}
    args = [nc.dram_tensor(n, a.shape, mybir.dt.from_np(a.dtype), kind="ExternalInput").ap()
            for n, a in arrays.items()]
    out = nc.dram_tensor("outT", xT.shape, F32, kind="ExternalOutput").ap()
    build(nc, *args, out)
    r = run_bass_kernel_spmd(nc, [arrays], core_ids=[0])
    y = r.results[0]["outT"].reshape(HALVES * TN, P, KT, NT)
    return y.transpose(0, 3, 2, 1).reshape(x.shape)
```

```python
from contextlib import ExitStack

import concourse.bass as bass
from concourse import mybir

F32 = mybir.dt.float32
F32R = mybir.dt.float32r
I32 = mybir.dt.int32
ALU = mybir.AluOpType
ACT = mybir.ActivationFunctionType
ds = bass.ds

P = 128
D = 1024
KT = D // P
MB = KT // 2
NT = 512
BT = 256
R = 16
HALVES = 2
TN = 2
HT = TN * NT
INTER = 2752
PAIRS = INTER // (2 * P)
NPAIR = PAIRS + 1
TAIL = INTER - PAIRS * 2 * P
LASTM = TAIL - P
TAILJ = TAIL // 2
GROUPS = 16
LORA_SCALE = 2.0
SLOTS = 32

X_CHUNKS = 4
UNITS = TN * KT
GU = NPAIR * 4
UP = GU - TN
DN = TN * KT
DH = NPAIR * DN
SP_PAIR = 6
STEPS = 4 + PAIRS * SP_PAIR + 2
CR = 4
STORE_K = 2
STORES = TN * KT // STORE_K
WARM_UP = 12


def build(nc, xT, idx, wT, bias, loraA, loraB, guq, gusz, dq, dsz, out):
    ctx = ExitStack()
    with ctx:
        def sb(name, shape, dt):
            return ctx.enter_context(nc.sbuf_tensor(name, shape, dt))

        def pb(name, shape):
            return ctx.enter_context(nc.psum_tensor(name, shape, F32))

        def sem(name):
            return ctx.enter_context(nc.semaphore(name))

        Ch = sb("Ch", [P, KT, HT], F32R)
        Cl = sb("Cl", [P, KT, HT], F32R)
        acc = sb("acc", [P, KT, HT], F32)
        Wh = sb("Wh", [P, 2, 2 * D], F32R)
        Wl = sb("Wl", [P, 2, 2 * D], F32R)
        Hh = sb("Hh", [P, 2 * TN * HT], F32R)
        Hl = sb("Hl", [P, 2 * TN * HT], F32R)
        raw = sb("raw", [P, 2, D], I32)
        sz = sb("sz", [P, 2, 2, 2, P], F32)
        rawd = sb("rawd", [P, D], I32)
        szd = sb("szd", [P, 2, D], F32)
        tmp = sb("tmp", [P, 2, D], F32)
        sg = sb("sg", [P, 2, NT], F32)
        hf = sb("hf", [P, 2, NT], F32)
        lh = sb("lh", [P, NT], F32R)
        araw = sb("araw", [P, 2, KT * R], F32)
        A = sb("A", [P, 2 * KT, 3 * R], F32R)
        unused = sb("unused", [P, 1], F32)
        bcol = sb("bcol", [P, KT], F32)

        pg = pb("pg", [P, 2, 2, NT])
        pd = pb("pd", [P, 4, NT])

        x_in = [sem(f"x_in{c}") for c in range(X_CHUNKS)]
        w_in = [sem(f"w_in{q}") for q in range(4)]
        gu_in = [sem(f"gu_in{q}") for q in range(2)]
        d_in = sem("d_in")
        a_in = sem("a_in")
        b_in = sem("b_in")
        acc_in = [sem(f"acc_in{n}") for n in range(TN)]
        bias_in = sem("bias_in")
        stored = sem("stored")
        acc_free = sem("acc_free")
        szd_zero = sem("szd_zero")
        lora_zero = sem("lora_zero")
        x_high = sem("x_high")
        a_high = sem("a_high")
        b_high = sem("b_high")
        w_high = sem("w_high")
        lh_high = sem("lh_high")
        c_high = sem("c_high")
        q_high = sem("q_high")
        h_high = sem("h_high")
        sig_done = sem("sig_done")
        set_loaded = sem("set_loaded")
        u_copied = sem("u_copied")
        x_split = sem("x_split")
        a_split = sem("a_split")
        b_split = sem("b_split")
        w_split = sem("w_split")
        lh_split = sem("lh_split")
        c_split = sem("c_split")
        gu_split = sem("gu_split")
        wd_split = sem("wd_split")
        h_split = sem("h_split")
        unpacked = sem("unpacked")
        centered = sem("centered")
        scaled = sem("scaled")
        silu_done = sem("silu_done")
        hf_done = sem("hf_done")
        added = sem("added")
        lora_mm = sem("lora_mm")
        c_mm = sem("c_mm")
        g_mm = sem("g_mm")
        u_mm = sem("u_mm")
        d_mm = sem("d_mm")

        block = ctx.enter_context(nc.Block())

        def f(ap):
            return ap.bitcast(F32)

        x_raw = [tmp[:, 0, :], tmp[:, 1, :], sg[:, :, :].rearrange("p s n -> p (s n)"),
                 hf[:, :, :].rearrange("p s n -> p (s n)")]

        def w_raw(n, o):
            return f(raw[:, o % 2, :]) if n < TN - 1 or o < 2 else x_raw[2 + o % 2]

        def w_landed(half, n, o):
            if n < TN - 1 or o < 2:
                return w_in[o % 2], (half * (MB + 1) + n * MB + o // 2 + 1) * 16
            return w_in[2 + o % 2], (half * (MB - 1) + o // 2) * 16

        def x_part(n, c):
            if n == 0 and c == 0:
                return Wl[:, 0, D:2 * D], Wl[:, 1, D:2 * D]
            return tuple(t[:, c * 2 * NT:(c + 1) * 2 * NT] for t in (Hh, Hl))

        def gu_part(t, slot, v):
            return t[:, slot, :].rearrange("p (g v n) -> p g v n", g=2, v=2)[:, :, v, :]

        def wd_part(t, tile):
            return t[:, TN * HT + tile * D:TN * HT + (tile + 1) * D]

        def h_part(t, tile, n, p0=0, p1=P):
            return t[p0:p1, tile * HT + n * NT:tile * HT + (n + 1) * NT]

        def step(j, i):
            return 4 + j * SP_PAIR + i

        @block.sync
        def _(sp):
            sp.dma_start(bcol[:, :], bias).then_inc(bias_in, 16)

            def load_gate_up(half, T, slot):
                sp.dma_start(raw[:, slot, :], guq[ds(T, 1), :, :].rearrange("t p n -> (t p) n"))\
                    .then_inc(gu_in[slot], 16)
                sp.dma_start(sz[:, slot, :, :, :].rearrange("p z g n -> p (z g n)"),
                             gusz[ds(T, 1), :, :].rearrange("t g n -> (t g) n").unsqueeze(1)
                             .broadcast_to([GROUPS, P // GROUPS, 4 * P])).then_inc(gu_in[slot], 16)

            def load_down(T):
                sp.dma_start(rawd[:, :], dq[ds(T, 1), :, :].rearrange("t p n -> (t p) n")).then_inc(d_in, 16)
                sp.dma_start(szd[:, :, :].rearrange("p z n -> p (z n)"),
                             dsz[ds(T, 1), :, :].rearrange("t g n -> (t g) n").unsqueeze(1)
                             .broadcast_to([4, P // 4, 2 * D])).then_inc(d_in, 16)

            def load_x(half, n, c, tile=None):
                tile = half * TN + n if tile is None else tile
                if n > 0:
                    sp.wait_ge(x_split, half * 2 * X_CHUNKS + c + 1)
                elif c < 2:
                    sp.wait_ge(wd_split, half * 2 * NPAIR + CR)
                else:
                    sp.wait_ge(h_split, half * GU + CR)
                sp.dma_start(x_raw[c], xT[ds(tile, 1), :, c * 2 * NT:(c + 1) * 2 * NT]
                             .rearrange("t p n -> (t p) n")).then_inc(x_in[c], 16)

            def load_w(half, n, o):
                i = n * KT + o
                if n == TN - 1 and o in (2, 3):
                    sp.wait_ge(x_split, half * 2 * X_CHUNKS + n * X_CHUNKS + o + 1)
                elif i >= 2:
                    sp.wait_ge(w_split, half * UNITS + i - 1)
                else:
                    sp.wait_ge(scaled, half * STEPS + CR)
                sp.dma_start(w_raw(n, o), wT[o, :, :]).then_inc(w_landed(half, n, o)[0], 16)

            load_x(0, 0, 0)
            load_w(0, 0, 0)
            with sp.Fori(0, HALVES) as half:
                def load_a(n):
                    if n > 0:
                        sp.wait_ge(a_split, half * TN + n)
                    for b in range(2):
                        sp.dma_start(araw[:, b, :], loraA[ds(adapters[n * 2 + b], 1), :, :]
                                     .rearrange("s p n -> (s p) n")).then_inc(a_in, 16)

                def load_b(n):
                    if n > 0:
                        sp.wait_ge(b_split, half * TN + n)
                    else:
                        sp.wait_ge(szd_zero, half + 1)
                    for b in range(2):
                        for r in range(0, P, 32):
                            sp.dma_start(szd[r:r + R, b, :], loraB[ds(adapters[n * 2 + b], 1), :, :]
                                         .rearrange("s p n -> (s p) n")).then_inc(b_in, 16)

                next_tile = sp.snap((half * TN + TN) % (HALVES * TN))
                load_x(half, 0, 1)
                adapters = [sp.value_load(idx[0:1, ds(half * TN * 2 + b, 1)], min_val=0, max_val=SLOTS - 1)
                            for b in range(TN * 2)]
                load_a(0)
                load_x(half, 0, 2)
                load_x(half, 0, 3)
                load_w(half, 0, 1)
                load_b(0)
                for o in range(2, 4):
                    load_w(half, 0, o)
                for c in range(X_CHUNKS):
                    load_x(half, 1, c)
                load_a(1)
                load_b(1)
                for o in range(4, KT):
                    load_w(half, 0, o)
                for o in range(4):
                    load_w(half, 1, o)
                for t in range(2):
                    sp.wait_ge(w_split, half * UNITS + KT + 1 + t)
                    load_gate_up(half, t, t)
                for o in range(4, KT):
                    load_w(half, 1, o)
                sp.wait_ge(b_split, half * TN + TN)
                load_down(0)
                sp.wait_ge(acc_free, half + 1)
                for n in reversed(range(TN)):
                    sp.dma_start(acc[:, :, n * NT:(n + 1) * NT],
                                 xT[ds(half * TN + n, 1), :, :].rearrange("t p (k c) -> (t p) k c", k=KT))\
                        .then_inc(acc_in[n], 16)
                with sp.Fori(0, PAIRS) as j:
                    for t in range(2):
                        sp.wait_ge(scaled, half * STEPS + j * SP_PAIR + 2 * t + 2 + CR)
                        load_gate_up(half, j * 2 + 2 + t, t)
                    sp.wait_ge(scaled, half * STEPS + step(j, 2) + CR)
                    load_down(j + 1)
                sp.wait_ge(scaled, half * STEPS + step(PAIRS, 1) + CR)
                load_down(NPAIR)
                load_x(half + 1, 0, 0, next_tile)
                load_w(half + 1, 0, 0)

        @block.gpsimd
        def _(pool):
            pool.memset(f(lh[:, :]), 0.0).then_inc(lora_zero, 1)
            pool.memset(f(A[:, :, :]), 0.0).then_inc(lora_zero, 1)
            pool.sem_inc(acc_free, 1)
            with pool.Fori(0, HALVES) as half:
                for n in range(TN):
                    for m0 in range(0, KT, STORE_K):
                        pool.wait_ge(added, half * DH + PAIRS * DN + n * KT + m0 + STORE_K + CR)
                        pool.wait_ge(added, CR)
                        pool.dma_start(out[ds(half * TN + n, 1), :, m0 * NT:(m0 + STORE_K) * NT]
                                       .rearrange("t p (k c) -> (t p) k c", k=STORE_K),
                                       acc[:, m0:m0 + STORE_K, n * NT:(n + 1) * NT]).then_inc(stored, 16)
                pool.wait_ge(stored, (half + 1) * STORES * 16)
                pool.sem_inc(acc_free, 1)
            pool.wait_ge(stored, HALVES * STORES * 16)

        @block.scalar
        def _(act):
            act.wait_ge(lora_zero, 2)
            act.activation(unused[0:1, :], f(lh[0:1, 0:1]), ACT.Sigmoid).then_inc(set_loaded, 1)
            act.wait_ge(set_loaded, 1)

            def round_to(dst, src, done, by=1):
                act.activation(dst, src, ACT.Copy).then_inc(done, by)

            def round_x(half, n, c):
                if n == 0:
                    if c == 0:
                        act.wait_ge(g_mm, half * GU + CR)
                    elif c == 1:
                        act.wait_ge(d_mm, half * DH + CR)
                elif c == 1:
                    act.wait_ge(c_mm, half * UNITS + KT)
                act.wait_ge(x_in[c], (half * TN + n + 1) * 16)
                round_to(x_part(n, c)[0], x_raw[c], x_high)

            def round_w(half, n, o):
                i = n * KT + o
                if i >= 2:
                    act.wait_ge(c_mm, half * UNITS + i - 1)
                elif i == 0:
                    act.wait_ge(g_mm, half * GU + CR)
                act.wait_ge(*w_landed(half, n, o))
                round_to(Wh[:, o % 2, 0:D], w_raw(n, o), w_high)

            round_x(0, 0, 0)
            round_w(0, 0, 0)
            with act.Fori(0, HALVES) as half:
                def round_a(n):
                    if n > 0:
                        act.wait_ge(lora_mm, half * TN + n)
                    act.wait_ge(a_in, (half * TN + n + 1) * 32)
                    round_to(A[:, :, 0:R], araw[:, :, :].rearrange("p b (k r) -> p (b k) r", r=R), a_high)

                def round_b(n):
                    act.wait_ge(b_in, (half * TN + n + 1) * 128)
                    for b in range(2):
                        round_to(Wh[:, b, D:2 * D], szd[:, b, :], b_high)

                def evac(n, o):
                    act.wait_ge(c_mm, half * UNITS + n * KT + o + 1)
                    act.activation(Ch[:, o, n * NT:(n + 1) * NT], pd[:, o % 4, :], ACT.Identity,
                                   bias=bcol[:, o:o + 1]).then_inc(c_high, 1)

                def evac_lora(n):
                    act.wait_ge(lora_mm, half * TN + n + 1)
                    for r, of in ((0, 0), (64, 0), (96, 32)):
                        act.activation(lh[r:r + R, :].rearrange("p (b n) -> p b n", b=2), pg[of:of + R, 0, :, 0:BT],
                                       ACT.Copy, scale=LORA_SCALE).then_inc(lh_high, 1)

                round_x(half, 0, 1)
                round_a(0)
                round_x(half, 0, 2)
                round_x(half, 0, 3)
                round_w(half, 0, 1)
                round_b(0)
                evac_lora(0)
                act.wait_ge(bias_in, 16)
                for o in range(KT - 2):
                    round_w(half, 0, o + 2)
                    evac(0, o)
                    if o == 3:
                        round_x(half, 1, 0)
                        round_a(1)
                evac(0, KT - 2)
                round_w(half, 1, 0)
                for c in range(1, X_CHUNKS):
                    round_x(half, 1, c)
                evac(0, KT - 1)
                round_w(half, 1, 1)
                round_b(1)
                evac_lora(1)
                for o in range(KT - 2):
                    round_w(half, 1, o + 2)
                    evac(1, o)
                evac(1, KT - 2)

                def round_q(v, dst, src):
                    act.wait_ge(scaled, half * STEPS + v + 1 + CR)
                    round_to(dst, src, q_high, 2)

                def round_gate_up(v0, t):
                    for v in range(2):
                        round_q(v0 + v, gu_part(Wh, t, v), tmp[:, v, :].rearrange("p (g n) -> p g n", g=2))

                def sigmoid(j, u):
                    act.wait_ge(g_mm, half * GU + j * 4 + u + 1 + CR)
                    act.activation(sg[:, u % 2, :], pg[:, u % 2, 0, :], ACT.Sigmoid).then_inc(sig_done, 1)

                def round_h(j, u):
                    act.wait_ge(hf_done, half * GU + j * 4 + u + 1)
                    round_to(h_part(Hh, u // 2, u % 2), hf[:, u % 2, :], h_high)

                for g in range(2):
                    act.wait_ge(c_mm, half * UNITS + UNITS - 1 + g)
                    for v in range(2):
                        act.wait_ge(scaled, half * STEPS + v + 1 + CR)
                        round_to(gu_part(Wh, 0, v)[:, g, :], tmp[:, v, g * NT:(g + 1) * NT], q_high)
                evac(1, KT - 1)
                round_gate_up(2, 1)

                with act.Fori(0, PAIRS) as j:
                    act.wait_ge(d_mm, half * DH + j * DN + CR)
                    round_q(step(j, 0), wd_part(Hh, 0), tmp[:, 0, :])
                    sigmoid(j, 0)
                    round_h(j, 0)
                    round_q(step(j, 1), wd_part(Hh, 1), tmp[:, 1, :])
                    sigmoid(j, 1)
                    round_h(j, 1)
                    act.wait_ge(u_mm, half * UP + j * 4 + 2)
                    round_gate_up(step(j, 2), 0)
                    sigmoid(j, 2)
                    round_h(j, 2)
                    sigmoid(j, 3)
                    round_h(j, 3)
                    act.wait_ge(u_mm, half * UP + j * 4 + 4)
                    round_gate_up(step(j, 4), 1)

                j = PAIRS
                act.wait_ge(d_mm, half * DH + j * DN + CR)
                round_q(step(j, 0), wd_part(Hh, 0), tmp[:, 0, :])
                sigmoid(j, 0)
                round_h(j, 0)
                round_q(step(j, 1), wd_part(Hh, 1), tmp[:, 1, :])
                sigmoid(j, 1)
                round_h(j, 1)
                for n in range(TN):
                    act.wait_ge(g_mm, half * GU + j * 4 + 2 + n + 1 + CR)
                    act.activation(sg[0:LASTM, n, :], pg[0:LASTM, n, 0, :], ACT.Sigmoid).then_inc(sig_done, 1)
                    act.activation(hf[0:LASTM, n, :], pg[LASTM:P, n, 0, :], ACT.Copy).then_inc(u_copied, 1)
                    act.wait_ge(hf_done, half * GU + j * 4 + 2 + n + 1)
                    round_to(h_part(Hh, 1, n, 0, LASTM), hf[0:LASTM, n, :], h_high)
                round_x(half + 1, 0, 0)
                round_w(half + 1, 0, 0)

        @block.vector
        def _(dve):
            dve.sem_inc(scaled, CR)
            dve.sem_inc(wd_split, CR)
            dve.sem_inc(added, CR)
            dve.sem_inc(h_split, CR)

            dve.memset(szd[:, :, :], 0.0).then_inc(szd_zero, 1)

            def low(dst, src, high, done, by=1):
                dve.tensor_tensor(dst, src, high, ALU.subtract).then_inc(done, by)

            def low_x(half, n, c):
                dve.wait_ge(x_high, half * 2 * X_CHUNKS + n * X_CHUNKS + c + 1)
                high, rest = x_part(n, c)
                low(rest, x_raw[c], f(high), x_split)

            def low_w(half, n, o):
                dve.wait_ge(w_high, half * UNITS + n * KT + o + 1)
                low(Wl[:, o % 2, 0:D], w_raw(n, o), f(Wh[:, o % 2, 0:D]), w_split)

            low_x(0, 0, 0)
            low_w(0, 0, 0)
            with dve.Fori(0, HALVES) as half:
                def unpack(parts, q, tmp_read):
                    dve.wait_ge(*tmp_read)
                    for i, (p0, p1, packed, high) in enumerate(parts):
                        dst = tmp[p0:p1, q, :].bitcast(I32)
                        if high:
                            ins = dve.tensor_scalar(dst, packed, 4, 15, ALU.arith_shift_right, ALU.bitwise_and)
                        else:
                            ins = dve.tensor_scalar(dst, packed, 15, None, ALU.bitwise_and)
                        if i == len(parts) - 1:
                            ins.then_inc(unpacked, 1)

                def center(v, zeros, shape, q):
                    dve.wait_ge(unpacked, half * STEPS + v + 1)
                    dve.tensor_tensor(shape(tmp[:, q, :]), shape(tmp[:, q, :].bitcast(I32)), zeros, ALU.subtract)\
                       .then_inc(centered, 1)

                def scale(v, scales, shape, q):
                    dve.wait_ge(centered, half * STEPS + v + 1)
                    dve.tensor_tensor(shape(tmp[:, q, :]), shape(tmp[:, q, :]), scales, ALU.mult).then_inc(scaled, 1)

                def flat(a):
                    return a

                def dequantise_down(v, parts, q, tmp_read):
                    unpack(parts, q, tmp_read)
                    center(v, szd[:, 0, :], flat, q)
                    scale(v, szd[:, 1, :], flat, q)

                def by_tile(a):
                    return a.rearrange("p (g m c) -> p g m c", g=2, m=MB)

                def gate_up_zs(slot, i):
                    return sz[:, slot, i, :, :].unsqueeze(2).broadcast_to([P, 2, MB, P])

                def dequantise_gate_up(v, slot, nib, landed, tmp_read):
                    if nib == 0:
                        dve.wait_ge(gu_in[slot], landed)
                    unpack([(0, P, raw[:, slot, :], nib == 0)], nib, tmp_read)
                    center(v, gate_up_zs(slot, 0), by_tile, nib)
                    scale(v, gate_up_zs(slot, 1), by_tile, nib)

                def low_gate_up(v, t, nib):
                    dve.wait_ge(q_high, half * 2 * STEPS + 2 * v + 2)
                    low(gu_part(Wl, t, nib), tmp[:, nib, :].rearrange("p (g n) -> p g n", g=2),
                        f(gu_part(Wh, t, nib)), gu_split, 2)

                def low_wd(v, tile):
                    dve.wait_ge(q_high, half * 2 * STEPS + 2 * v + 2)
                    low(wd_part(Hl, tile), tmp[:, tile, :], f(wd_part(Hh, tile)), wd_split)

                def low_a(n):
                    dve.wait_ge(a_high, half * TN + n + 1)
                    low(A[:, :, 2 * R:3 * R], araw[:, :, :].rearrange("p b (k r) -> p (b k) r", r=R),
                        f(A[:, :, 0:R]), a_split)

                def low_b(n):
                    dve.wait_ge(b_high, (half * TN + n + 1) * 2)
                    low(Wh[64:64 + R, :, D:2 * D], szd[64:64 + R, :, :], f(Wh[64:64 + R, :, D:2 * D]), b_split)

                def low_lora(n):
                    dve.wait_ge(lh_high, (half * TN + n + 1) * 3)
                    dve.scalar_tensor_tensor(lh[32:32 + R, :].rearrange("p (b n) -> p b n", b=2),
                                             pg[0:R, 0, :, 0:BT], LORA_SCALE,
                                             f(lh[0:R, :]).rearrange("p (b n) -> p b n", b=2),
                                             op0=ALU.mult, op1=ALU.subtract).then_inc(lh_split, 1)

                def low_c(n, o):
                    dve.wait_ge(c_high, half * UNITS + n * KT + o + 1)
                    dve.scalar_tensor_tensor(Cl[:, o, n * NT:(n + 1) * NT], pd[:, o % 4, :],
                                             bcol[:, o:o + 1], f(Ch[:, o, n * NT:(n + 1) * NT]),
                                             op0=ALU.add, op1=ALU.subtract).then_inc(c_split, 1)

                low_x(half, 0, 1)
                low_a(0)
                low_x(half, 0, 2)
                low_x(half, 0, 3)
                low_w(half, 0, 1)
                low_b(0)
                low_lora(0)
                for o in range(KT - 2):
                    low_w(half, 0, o + 2)
                    low_c(0, o)
                    if o == 3:
                        low_x(half, 1, 0)
                        low_a(1)
                low_c(0, KT - 2)
                low_w(half, 1, 0)
                for c in range(1, X_CHUNKS):
                    low_x(half, 1, c)
                low_c(0, KT - 1)
                low_w(half, 1, 1)
                low_b(1)
                low_lora(1)
                first = (half * NPAIR + 1) * 32
                for o in range(KT - 2):
                    low_w(half, 1, o + 2)
                    low_c(1, o)
                    if o in (2, 3):
                        dequantise_gate_up(o - 2, 0, o - 2, first,
                                           (x_split, half * 2 * X_CHUNKS + X_CHUNKS + o - 1))
                for g in range(2):
                    for v in range(2):
                        dve.wait_ge(q_high, half * 2 * STEPS + g * 2 + v + 1)
                        low(gu_part(Wl, 0, v)[:, g, :], tmp[:, v, g * NT:(g + 1) * NT],
                            f(gu_part(Wh, 0, v)[:, g, :]), gu_split)
                low_c(1, KT - 2)
                low_c(1, KT - 1)
                dequantise_gate_up(2, 1, 0, first, (gu_split, half * 2 * GU + 3))
                dequantise_gate_up(3, 1, 1, first, (gu_split, half * 2 * GU + 4))
                low_gate_up(2, 1, 0)
                low_gate_up(3, 1, 1)

                def make_h(j, u):
                    s = u % 2
                    dve.wait_ge(sig_done, half * GU + j * 4 + u + 1)
                    dve.tensor_tensor(sg[:, s, :], pg[:, s, 0, :], sg[:, s, :], ALU.mult).then_inc(silu_done, 1)
                    dve.wait_ge(u_mm, half * UP + j * 4 + u + 1)
                    dve.wait_ge(silu_done, half * GU + j * 4 + u + 1)
                    dve.tensor_tensor(hf[:, s, :], pg[:, s, 1, :], sg[:, s, :], ALU.mult).then_inc(hf_done, 1)

                def low_h(j, u):
                    dve.wait_ge(h_high, half * GU + j * 4 + u + 1)
                    low(h_part(Hl, u // 2, u % 2), hf[:, u % 2, :], f(h_part(Hh, u // 2, u % 2)), h_split)

                def add(j, n, m):
                    i = n * KT + m
                    if m == 0:
                        dve.wait_ge(acc_in[n], (half + 1) * 16)
                    dve.wait_ge(d_mm, half * DH + j * DN + i + 1 + CR)
                    a = acc[:, m, n * NT:(n + 1) * NT]
                    dve.tensor_tensor(a, a, pd[:, i % 4, :], ALU.add).then_inc(added, 1)

                with dve.Fori(0, PAIRS) as j:
                    dve.wait_ge(d_in, (half * (NPAIR + 1) + j + 1) * 32)
                    dequantise_down(step(j, 0), [(0, P, rawd[:, :], True)], 0,
                                    (gu_split, half * 2 * GU + j * 8 + 6))
                    low_wd(step(j, 0), 0)
                    make_h(j, 0)
                    low_h(j, 0)
                    dequantise_down(step(j, 1), [(0, P, rawd[:, :], False)], 1,
                                    (gu_split, half * 2 * GU + j * 8 + 8))
                    low_wd(step(j, 1), 1)
                    make_h(j, 1)
                    low_h(j, 1)
                    landed = (half * NPAIR + j + 2) * 32
                    dequantise_gate_up(step(j, 2), 0, 0, landed, (wd_split, half * 2 * NPAIR + 2 * j + 1 + CR))
                    dequantise_gate_up(step(j, 3), 0, 1, landed, (wd_split, half * 2 * NPAIR + 2 * j + 2 + CR))
                    low_gate_up(step(j, 2), 0, 0)
                    low_gate_up(step(j, 3), 0, 1)
                    make_h(j, 2)
                    low_h(j, 2)
                    dequantise_gate_up(step(j, 4), 1, 0, landed, (gu_split, half * 2 * GU + j * 8 + 10))
                    make_h(j, 3)
                    low_h(j, 3)
                    for n in range(TN):
                        for m in range(KT):
                            add(j, n, m)
                            i = n * KT + m
                            if i == 0:
                                unpack([(0, P, raw[:, 1, :], False)], 1, (gu_split, half * 2 * GU + j * 8 + 12))
                            elif i == 2:
                                center(step(j, 5), gate_up_zs(1, 0), by_tile, 1)
                            elif i == 4:
                                scale(step(j, 5), gate_up_zs(1, 1), by_tile, 1)
                            elif i == 6:
                                low_gate_up(step(j, 4), 1, 0)
                            elif i == 8:
                                low_gate_up(step(j, 5), 1, 1)

                j = PAIRS
                dve.wait_ge(d_in, (half * (NPAIR + 1) + j + 1) * 32)
                dequantise_down(step(j, 0), [(0, TAILJ, rawd[0:TAILJ, :], True), (TAILJ, P, rawd[TAILJ:P, :], False)], 0,
                                    (gu_split, half * 2 * GU + 2 * GU - 2))
                low_wd(step(j, 0), 0)
                make_h(j, 0)
                low_h(j, 0)
                dve.wait_ge(d_in, (half * (NPAIR + 1) + j + 2) * 32)
                dequantise_down(step(j, 1), [(0, P, rawd[:, :], False)], 1,
                                    (gu_split, half * 2 * GU + 2 * GU))
                low_wd(step(j, 1), 1)
                make_h(j, 1)
                low_h(j, 1)
                dve.wait_ge(scaled, half * STEPS + STEPS + CR)
                dve.memset(szd[:, :, :], 0.0).then_inc(szd_zero, 1)
                for n in range(TN):
                    i = half * GU + j * 4 + 2 + n + 1
                    dve.wait_ge(sig_done, i)
                    dve.tensor_tensor(sg[0:LASTM, n, :], pg[0:LASTM, n, 0, :], sg[0:LASTM, n, :], ALU.mult)\
                       .then_inc(silu_done, 1)
                    dve.wait_ge(silu_done, i)
                    dve.wait_ge(u_copied, half * TN + n + 1)
                    dve.tensor_tensor(hf[0:LASTM, n, :], hf[0:LASTM, n, :], sg[0:LASTM, n, :], ALU.mult)\
                       .then_inc(hf_done, 1)
                    dve.wait_ge(h_high, i)
                    low(h_part(Hh, 1, n, LASTM, P), hf[0:LASTM, n, :], f(h_part(Hh, 1, n, 0, LASTM)), h_split)
                for n in range(TN):
                    for m in range(KT):
                        add(j, n, m)
                        if n == 0 and m == 1:
                            low_x(half + 1, 0, 0)
                        elif n == 0 and m == 5:
                            low_w(half + 1, 0, 0)

        @block.tensor
        def _(pe):
            pe.sem_inc(d_mm, CR)
            pe.sem_inc(g_mm, CR)
            pe.wait_ge(lora_zero, 1)
            for _ in range(WARM_UP):
                pe.matmul(pd[:, 3, :], lh[:, 0:P], lh[:, :], start=True, stop=True)

            with pe.Fori(0, HALVES) as half:
                def lora_in(n, c):
                    for k in (2 * c, 2 * c + 1):
                        for b in range(2):
                            cols = slice((k % 2) * NT + b * BT, (k % 2) * NT + (b + 1) * BT)
                            xh, xl = (t[:, cols] for t in x_part(n, c))
                            pe.matmul(pg[0:3 * R, 0, b, 0:BT], A[:, b * KT + k, :], xh, start=(k == 0), stop=False)
                            last = pe.matmul(pg[0:3 * R, 0, b, 0:BT], A[:, b * KT + k, :], xl, start=False,
                                             stop=(k == KT - 1))
                    return last

                def lora_out(m):
                    for b in range(2):
                        pe.matmul(pd[:, m % 4, b * BT:(b + 1) * BT], Wh[:, b, D + m * P:D + (m + 1) * P],
                                  lh[:, b * BT:(b + 1) * BT], start=False, stop=False)

                def cond_unit(n, m, c):
                    for k in (2 * c, 2 * c + 1):
                        wh, wl = (t[:, m % 2, k * P:(k + 1) * P] for t in (Wh, Wl))
                        xh, xl = (t[:, (k % 2) * NT:(k % 2 + 1) * NT] for t in x_part(n, c))
                        if k == KT - 1:
                            lora_out(m)
                        pe.matmul(pd[:, m % 4, :], wh, xh, start=(k == 0), stop=False)
                        pe.matmul(pd[:, m % 4, :], wh, xl, start=False, stop=False)
                        last = pe.matmul(pd[:, m % 4, :], wl, xh, start=False, stop=(k == KT - 1))
                    return last

                def unit_may_start(n, m):
                    i = n * KT + m
                    if i < 4:
                        pe.wait_ge(added, half * DH + i - 3 + CR)
                    else:
                        pe.wait_ge(c_split, half * UNITS + i - 3)
                    pe.wait_ge(w_split, half * UNITS + i + 1)

                for n in range(TN):
                    def x_ready(c):
                        pe.wait_ge(x_split, half * 2 * X_CHUNKS + n * X_CHUNKS + c + 1)

                    def lora_may_start():
                        pe.wait_ge(h_split, half * GU + CR)
                        pe.wait_ge(a_split, half * TN + n + 1)

                    unit_may_start(n, 0)
                    x_ready(0)
                    cond_unit(n, 0, 0)
                    if n == 0:
                        x_ready(1)
                        cond_unit(n, 0, 1)
                        lora_may_start()
                        lora_in(n, 0)
                        lora_in(n, 1)
                    else:
                        lora_may_start()
                        lora_in(n, 0)
                        x_ready(1)
                        cond_unit(n, 0, 1)
                        lora_in(n, 1)
                    x_ready(2)
                    lora_in(n, 2)
                    x_ready(3)
                    lora_in(n, 3).then_inc(lora_mm, 1)
                    cond_unit(n, 0, 2)
                    unit_may_start(n, 1)
                    for c in range(2):
                        cond_unit(n, 1, c)
                    pe.wait_ge(b_split, half * TN + n + 1)
                    pe.wait_ge(lh_split, half * TN + n + 1)
                    cond_unit(n, 0, 3).then_inc(c_mm, 1)
                    for c in range(2, 4):
                        last = cond_unit(n, 1, c)
                    last.then_inc(c_mm, 1)
                    for m in range(2, KT):
                        unit_may_start(n, m)
                        for c in range(X_CHUNKS):
                            last = cond_unit(n, m, c)
                        last.then_inc(c_mm, 1)

                def project(j, t, n, g):
                    o = pg[:, n, g, :]
                    for k in range(KT):
                        if g == 0 and n == 0 and k % MB == 0:
                            pe.wait_ge(gu_split, half * 2 * GU + j * 8 + t * 4 + (k // MB + 1) * 2)
                        wh, wl = (w[:, t, g * D + k * P:g * D + (k + 1) * P] for w in (Wh, Wl))
                        cs = slice(n * NT, (n + 1) * NT)
                        pe.matmul(o, wh, Ch[:, k, cs], start=(k == 0), stop=False)
                        pe.matmul(o, wh, Cl[:, k, cs], start=False, stop=False)
                        last = pe.matmul(o, wl, Ch[:, k, cs], start=False, stop=(k == KT - 1))
                    return last

                def gate_up_unit(j, t, n):
                    u = t * TN + n
                    pe.wait_ge(h_split, half * GU + j * 4 + u - 1 + CR)
                    if t == 0:
                        pe.wait_ge(c_split, half * UNITS + (n + 1) * KT)
                    project(j, t, n, 0).then_inc(g_mm, 1)
                    project(j, t, n, 1).then_inc(u_mm, 1)

                def down(j, terms):
                    for n in range(TN):
                        pe.wait_ge(h_split, half * GU + j * 4 + 3 + n + CR)
                        if n == 0:
                            pe.wait_ge(wd_split, half * 2 * NPAIR + j * 2 + 2 + CR)
                        for m in range(KT):
                            i = n * KT + m
                            pe.wait_ge(added, half * DH + j * DN + i - 3 + CR)
                            for a, (w, h, tile) in enumerate(terms):
                                lo = TN * HT + tile * D + m * P
                                last = pe.matmul(pd[:, i % 4, :], w[:, lo:lo + P], h_part(h, tile, n),
                                                 start=(a == 0), stop=(a == len(terms) - 1))
                            last.then_inc(d_mm, 1)

                with pe.Fori(0, PAIRS) as j:
                    for t in range(2):
                        for n in range(TN):
                            gate_up_unit(j, t, n)
                    down(j, [(w, h, t) for t in range(2) for w, h in ((Hh, Hh), (Hh, Hl), (Hl, Hh))])

                j = PAIRS
                for n in range(TN):
                    gate_up_unit(j, 0, n)
                for n in range(TN):
                    pe.wait_ge(h_split, half * GU + j * 4 + 2 + n - 1 + CR)
                    project(j, 1, n, 0).then_inc(g_mm, 1)
                down(j, [(Hh, Hh, 0), (Hh, Hl, 0), (Hl, Hh, 0), (Hh, Hh, 1), (Hl, Hh, 1)])


def kernel(x, itok_B_0_23, L0_cond_W, L0_cond_b, L0_cond_lora_As, L0_cond_lora_Bs,
           L0_ffn_gate_Wq, L0_ffn_up_Wq, L0_ffn_down_Wq, L0_ffn_gate_scale, L0_ffn_gate_zero,
           L0_ffn_up_scale, L0_ffn_up_zero, L0_ffn_down_scale, L0_ffn_down_zero):
    import numpy as np
    import concourse.bacc as bacc
    from concourse.bass_utils import run_bass_kernel_spmd

    def c_rows(a):
        a = a.reshape(*a.shape[:-1], GROUPS, MB, 8, 2)
        lead = tuple(range(a.ndim - 4))
        return a.transpose(*lead, *(len(lead) + i for i in (3, 1, 0, 2)))

    def inter_tiles(a):
        main = a[:PAIRS * 2 * P].reshape(PAIRS, P, 2, -1).transpose(0, 2, 1, 3).reshape(2 * PAIRS, P, -1)
        tail = a[PAIRS * 2 * P:].reshape(TAILJ, 2, -1)
        return [*main, np.concatenate([tail[:, 0], tail[:P - TAILJ, 1]]), tail[P - TAILJ:, 1]]

    def gate_up(g, u):
        g, u = inter_tiles(g), inter_tiles(u)
        last = np.concatenate([g[-1], u[-1]])
        return np.stack([np.stack([a, b]) for a, b in zip(g[:-1], u[:-1])] + [np.stack([last, last])])

    x = np.asarray(x)
    xT = x.reshape(HALVES * TN, NT, KT, P).transpose(0, 3, 2, 1).reshape(HALVES * TN, P, KT * NT)
    W = np.asarray(L0_cond_W)
    wT = c_rows(W.T).reshape(KT, P, 2 * MB, P).transpose(2, 1, 0, 3).reshape(KT, P, D)
    bias = c_rows(np.asarray(L0_cond_b)).reshape(KT, P).T
    loraA = np.asarray(L0_cond_lora_As).reshape(SLOTS, KT, P, R).transpose(0, 2, 1, 3).reshape(SLOTS, P, KT * R)
    loraB = c_rows(np.asarray(L0_cond_lora_Bs)).reshape(SLOTS, R, D)
    guq = gate_up(np.asarray(L0_ffn_gate_Wq), np.asarray(L0_ffn_up_Wq))
    guq = guq.reshape(-1, 2, P, GROUPS, MB, 8).transpose(0, 3, 5, 1, 4, 2).reshape(-1, P, D)
    gz = gate_up(np.asarray(L0_ffn_gate_zero), np.asarray(L0_ffn_up_zero))
    gs = gate_up(np.asarray(L0_ffn_gate_scale), np.asarray(L0_ffn_up_scale))
    gusz = np.stack([gz, gs], axis=1).transpose(0, 4, 1, 2, 3).reshape(-1, GROUPS, 4 * P)
    dqT = np.asarray(L0_ffn_down_Wq).T
    tail = dqT[PAIRS * P:]
    dq = np.concatenate([dqT[:PAIRS * P].reshape(PAIRS, P, D),
                         np.concatenate([tail, tail[:P - TAILJ]])[None],
                         np.concatenate([tail[P - TAILJ:], tail[P - TAILJ:]])[None]])
    z, s = np.asarray(L0_ffn_down_zero).T, np.asarray(L0_ffn_down_scale).T
    zs = np.stack([z, s], axis=1).reshape(-1, 2 * D)
    t = 4 * PAIRS
    dsz = np.concatenate([zs[:t].reshape(PAIRS, 4, 2 * D), np.stack([zs[t], zs[t + 1], zs[t + 2], zs[t]])[None],
                          np.stack([zs[t + 1], zs[t + 2], zs[t + 1], zs[t + 2]])[None]])

    nc = bacc.Bacc("TRN2", target_bir_lowering=False, num_devices=1)
    arrays = {"xT": xT, "idx": np.asarray(itok_B_0_23).reshape(1, -1), "wT": wT, "bias": bias, "loraA": loraA,
              "loraB": loraB, "guq": guq, "gusz": gusz, "dq": dq, "dsz": dsz}
    arrays = {n: np.ascontiguousarray(a) for n, a in arrays.items()}
    args = [nc.dram_tensor(n, a.shape, mybir.dt.from_np(a.dtype), kind="ExternalInput").ap()
            for n, a in arrays.items()]
    out = nc.dram_tensor("outT", xT.shape, F32, kind="ExternalOutput").ap()
    build(nc, *args, out)
    r = run_bass_kernel_spmd(nc, [arrays], core_ids=[0])
    y = r.results[0]["outT"].reshape(HALVES * TN, P, KT, NT)
    return y.transpose(0, 3, 2, 1).reshape(x.shape)
```
